# Optimizing a Trainium2 kernel written in Bass

```python
import numpy as np
import jax
import jax.numpy as jnp

def _softmax(x, axis=-1):
    return jax.nn.softmax(x, axis=axis)
def _gelu(x):
    return jax.nn.gelu(x, approximate=True)
def _silu(x):
    return jax.nn.silu(x)
def _sigmoid(x):
    return jax.nn.sigmoid(x)
def _layernorm(x, axis=-1, eps=1e-5):
    m = jnp.mean(x, axis=axis, keepdims=True)
    v = jnp.var(x, axis=axis, keepdims=True)
    return (x - m) / jnp.sqrt(v + eps)
def _scatter_add(tgt, idx, src, axis=0):
    return tgt.at[idx].add(src)
def _segment_sum(src, seg, n):
    return jax.ops.segment_sum(src, seg, n)

kernel_name = 'mk_adj_preln_d1_adj_64_8ca4f5'

def setup_inputs(seed: int = 0):
    np.random.seed(seed)
    _w = jnp.asarray
    def _rec_inputs():
        import jax
        import jax.numpy as jnp
        _gk = jax.random.key(seed)
        x = -9.806e-05 + 1 * jax.random.normal(jax.random.fold_in(_gk, 1), (4096, 64), jnp.float32)
        _a = jax.random.bernoulli(jax.random.fold_in(_gk, 2), 0.0078125, (4096, 4096))
        _af = _a.astype(jnp.float32)
        adj = _af
        return x, adj
    x, adj = _rec_inputs()
    def _L0_gnn_setup():
        import jax, jax.numpy as jnp
        import numpy as np
        N, D_IN, D_OUT = (8192, 64, 64)
        MAX_NEIGH = 100
        DECAY = 0.5
        key = jax.random.key(seed)
        k1, k2, k3, k4 = jax.random.split(key, 4)
        stdv = 1.0 / np.sqrt(D_OUT)
        inputs = {'input': jax.random.normal(k1, (N, D_IN), dtype=jnp.float32), 'adj': jax.random.randint(k2, (N, N), 0, 2).astype(jnp.float32), 'weight': jax.random.uniform(k3, (D_IN, D_OUT), minval=-stdv, maxval=stdv, dtype=jnp.float32), 'bias': jax.random.uniform(k4, (D_OUT,), minval=-stdv, maxval=stdv, dtype=jnp.float32)}
        return inputs
    _L0_gnn_all = _L0_gnn_setup()
    _L0_gnn_in = {k: v for k, v in _L0_gnn_all.items() if k in ('weight', 'bias', )}
    del _L0_gnn_all

    return {
        "x": x,
        "adj": adj,
        "L0_gnn_weight": _L0_gnn_in["weight"],
        "L0_gnn_bias": _L0_gnn_in["bias"],
    }

def reference(x, adj, L0_gnn_weight, L0_gnn_bias):
    import jax
    import jax.numpy as jnp
    def _L0_gnn_ref(input, adj, weight, bias):
        import jax, jax.numpy as jnp
        import numpy as np
        N, D_IN, D_OUT = (8192, 64, 64)
        MAX_NEIGH = 100
        DECAY = 0.5
        support = input @ weight
        mask = (adj != 0).astype(support.dtype)
        rank = jnp.cumsum(mask, axis=1)
        deg = rank[:, -1:]
        k = jnp.minimum(deg, float(MAX_NEIGH))
        pos = rank - (deg - k)
        w = mask * jnp.where(pos > 0, DECAY ** (k - pos), 0.0)
        out = w @ support + bias
        return out

    h = jnp.maximum(_layernorm(x, axis=-1), 0.0)
    x = x + _L0_gnn_ref(h, adj, L0_gnn_weight, L0_gnn_bias)
    return x


_drawn_inputs = setup_inputs


def setup_inputs(seed=0):
    import zlib

    import numpy as np

    out = dict(_drawn_inputs(seed))
    spreads = {}
    factors = {}
    for name, (base, spread) in spreads.items():
        noise = np.random.default_rng([zlib.crc32(name.encode()), seed]).standard_normal(out[name].shape)
        drawn = base * np.exp(spread * noise) if base else spread * noise
        out[name] = jnp.asarray(drawn.astype(out[name].dtype))
    for name, factor in factors.items():
        out[name] = (out[name] * factor).astype(out[name].dtype)
    return out
```

```python
from contextlib import ExitStack

import concourse.bass as bass
from concourse import mybir

ALU = mybir.AluOpType
ACT = mybir.ActivationFunctionType
AX = mybir.AxisListType
F32 = mybir.dt.float32
F16 = mybir.dt.float16
BF16 = mybir.dt.bfloat16
FP8 = mybir.dt.float8e4
I16 = mybir.dt.int16
I32 = mybir.dt.int32
U32 = mybir.dt.uint32

P = 128
MAX_NEIGH = 100
EXP_ONE = 128
BF16_BIAS = 127
BIAS = MAX_NEIGH * EXP_ONE
DROP = 16384
EPS = 1e-5
HALF_BITS = 11
SUP_BITS = 10
OUT_BITS = BF16_BIAS - MAX_NEIGH
LN_BOUND_FLOOR = 2.0 ** -100


def neighbour_decay_kernel(nc, x, adj, weight, bias, out):
    N, D = x.shape
    TILES = N // P
    CH = 2
    CT = 4
    ROWS = CT * P
    EB = 4
    COLS = EB * P
    UNITS = N // COLS
    GROUPS = N // (CH * ROWS)
    RING = 4
    PAIRS = TILES // 2
    assert D == 64 and TILES == 32 and UNITS == 8 and UNITS % RING == 0

    adj_v = adj.rearrange("(g h t p) j -> g h p t j", h=CH, t=CT, p=P)
    x_v = x.rearrange("(t p) d -> p t d", p=P)
    out_v = out.rearrange("(g h t p) d -> g h p t d", h=CH, t=CT, p=P)
    bias_v = bias.rearrange("(a d) -> a d", a=1)

    with ExitStack() as ctx:
        def sb(name, shape, dt):
            return ctx.enter_context(nc.sbuf_tensor(name, shape, dt))

        def psum(name):
            return ctx.enter_context(nc.psum_tensor(name, [P, 512], F32))

        def sem(name):
            return ctx.enter_context(nc.semaphore(name))

        adj_ring = sb("adj_ring", [P, RING, CH, CT, COLS], F32)
        mask = sb("mask", [P, 2, CH, CT, COLS], FP8)
        mask_t = sb("mask_t", [P, 2, CH, ROWS, EB], FP8)
        wts = sb("wts", [P, CH, 2 * EB, ROWS], I16)
        acc_sb = sb("acc_sb", [P, CH, ROWS], F32)
        out_sb = sb("out_sb", [P, CH, CT, D], F32)
        ident = sb("ident", [P, P], F32)
        ones = sb("ones", [P, P], F32)
        this_block = sb("this_block", [P, P], BF16)
        to_left = sb("to_left", [P, P], BF16)
        unscale = sb("unscale", [P, D], F32)
        xs = sb("xs", [P, TILES, D], F32)
        bias_sb = sb("bias_sb", [P, D], F32)
        x_bias = sb("x_bias", [P, TILES, D], F32)
        cen = sb("cen", [P, TILES, D], F32)
        sq = sb("sq", [P, TILES, D], F32)
        row_sum = sb("row_sum", [P, TILES], F32)
        mean = sb("mean", [P, TILES], F32)
        sq_sum = sb("sq_sum", [P, TILES], F32)
        var = sb("var", [P, TILES], F32)
        std = sb("std", [P, TILES], F32)
        rstd0 = sb("rstd0", [P, TILES], F32)
        nw1 = sb("nw1", [P, TILES], F32)
        nw2 = sb("nw2", [P, TILES], F32)
        nw3 = sb("nw3", [P, TILES], F32)
        rstd = sb("rstd", [P, TILES], F32)
        h_sb = sb("h_sb", [P, TILES, D], F32)
        h_t = sb("h_t", [P, PAIRS, P], F32)
        w2 = sb("w2", [P, P], F32)
        w2_abs = sb("w2_abs", [P, P], F32)
        w2_sc = sb("w2_sc", [P, P], F32)
        bound = sb("bound", [P, P], F32)
        pow2 = sb("pow2", [P, P], F32)
        inv2 = sb("inv2", [P, P], F32)
        rest = sb("rest", [P, TILES, D], F32)
        support = sb("support", [P, TILES, 2, D], F16)

        words_ps = [psum(f"words_ps{h}") for h in range(CH)]
        count_ps = [psum(f"count_ps{h}") for h in range(CH)]
        acc_ps = [psum(f"acc_ps{h}") for h in range(CH)]
        rows_ps = [psum(f"rows_ps{h}") for h in range(CH)]

        load_done = [[sem(f"load_done{r}_{h}") for h in range(CH)] for r in range(RING)]
        x_loaded = sem("x_loaded")
        w_loaded = sem("w_loaded")
        bias_loaded = sem("bias_loaded")
        pool_step = sem("pool_step")
        ident_set = sem("ident_set")
        count_mats_set = sem("count_mats_set")
        unscale_set = sem("unscale_set")
        ones_set = sem("ones_set")
        w2_cleared = sem("w2_cleared")
        x_bias_set = sem("x_bias_set")
        mean_set = sem("mean_set")
        centred = sem("centred")
        squared = sem("squared")
        var_set = sem("var_set")
        std_set = sem("std_set")
        h_set = sem("h_set")
        w_abs_set = sem("w_abs_set")
        bound_ready = sem("bound_ready")
        w_scaled = sem("w_scaled")
        unscale_ready = sem("unscale_ready")
        h_turned = sem("h_turned")
        h_t_set = sem("h_t_set")
        support_ready = sem("support_ready")
        high_set = sem("high_set")
        rest_set = sem("rest_set")
        support_set = sem("support_set")
        dve_step = sem("dve_step")
        mask_ready = [sem(f"mask_ready{h}") for h in range(CH)]
        words_ready = [sem(f"words_ready{h}") for h in range(CH)]
        mask_t_ready = [sem(f"mask_t_ready{h}") for h in range(CH)]
        count_ready = [sem(f"count_ready{h}") for h in range(CH)]
        wts_ready = [sem(f"wts_ready{h}") for h in range(CH)]
        product_done = [sem(f"product_done{h}") for h in range(CH)]
        acc_copied = [sem(f"acc_copied{h}") for h in range(CH)]
        rows_ready = [sem(f"rows_ready{h}") for h in range(CH)]
        out_ready = [sem(f"out_ready{h}") for h in range(CH)]
        out_stored = [sem(f"out_stored{h}") for h in range(CH)]

        def wait_apart(eng, s, value):
            eng.wait_ge(s, value)
            if not isinstance(value, int):
                eng.sem_inc(waits_carried, 1)

        def ht_ps(q):
            return acc_ps[q % 2]

        def sup_ps(q):
            return rows_ps[q % 2]

        waits_carried = sem("waits_carried")

        block = ctx.enter_context(nc.Block())

        @block.sync
        def _(sp):
            def load(g, c, again):
                for h in range(CH):
                    if again:
                        wait_apart(sp, mask_ready[h], UNITS * g + c - RING + 1)
                    j0 = N - COLS * (c + 1)
                    sp.dma_start(adj_ring[:, c % RING, h], adj_v[g, h, :, :, j0:j0 + COLS])\
                      .then_inc(load_done[c % RING][h], 16)

            for c in range(UNITS):
                load(0, c, c >= RING)
            with sp.Fori(1, GROUPS) as g:
                for c in range(UNITS):
                    load(g, c, True)

        @block.gpsimd
        def _(pool):
            steps = [0]

            def then_next(ins):
                steps[0] += 1
                ins.then_inc(pool_step, 1)
                pool.wait_ge(pool_step, steps[0])

            def fill_where(t, keep, base, step, cm, fill):
                return nc.gpsimd.affine_select(out=t, in_=t, compare_op=keep, fill=fill, base=base,
                                               pattern=[[step, t.shape[1]]], channel_multiplier=cm)

            nc.gpsimd.memset(w2[:], 0.0).then_inc(w2_cleared, 1)
            then_next(nc.gpsimd.memset(ident[:], 0.0))
            fill_where(ident[:], ALU.not_equal, 0, -1, 1, 1.0).then_inc(ident_set, 1)
            then_next(nc.gpsimd.memset(this_block[:], 0.0))
            then_next(fill_where(this_block[:], ALU.is_ge, 0, 1, -1, float(-EXP_ONE)))
            then_next(fill_where(this_block[:], ALU.not_equal, 0, 1, -1, float(DROP)))
            then_next(nc.gpsimd.memset(to_left[:], float(-EXP_ONE)))
            then_next(fill_where(to_left[:], ALU.is_ge, 0, 1, -1, 0.0))
            fill_where(to_left[:], ALU.not_equal, 0, 1, -1, float(-EXP_ONE - DROP)).then_inc(count_mats_set, 1)
            nc.gpsimd.memset(ones[:], 1.0).then_inc(ones_set, 1)
            then_next(nc.gpsimd.memset(unscale[:], 0.0))
            then_next(fill_where(unscale[:], ALU.not_equal, 0, -1, 1, 2.0 ** (OUT_BITS - SUP_BITS)))
            fill_where(unscale[:], ALU.not_equal, -D, -1, 1,
                       2.0 ** (OUT_BITS - SUP_BITS - HALF_BITS)).then_inc(unscale_set, 1)
            pool.wait_ge(x_loaded, 16)
            pool.wait_ge(mean_set, 1)
            nc.gpsimd.tensor_tensor(cen[:], xs[:], mean[:].unsqueeze(2).broadcast_to([P, TILES, D]),
                                    ALU.subtract).then_inc(centred, 1)
            pool.wait_ge(bias_loaded, 16)
            nc.gpsimd.tensor_tensor(x_bias[:], xs[:], bias_sb[:].unsqueeze(1).broadcast_to([P, TILES, D]),
                                    ALU.add).then_inc(x_bias_set, 1)
            with pool.Fori(0, GROUPS) as g:
                for h in range(CH):
                    pool.wait_ge(out_ready[h], g + 1)
                    pool.dma_start(out_v[g, h], out_sb[:, h]).then_inc(out_stored[h], 16)
            for h in range(CH):
                pool.wait_ge(out_stored[h], 16 * GROUPS)

        @block.scalar
        def _(act):
            act.dma_start(xs[:], x_v).then_inc(x_loaded, 16)
            act.wait_ge(w2_cleared, 1)
            act.dma_start(w2[0:D, 0:D], weight).then_inc(w_loaded, 16)
            act.dma_start(w2[D:P, D:P], weight).then_inc(w_loaded, 16)
            act.dma_start(bias_sb[:], bias_v.broadcast_to([P, D])).then_inc(bias_loaded, 16)

            def weights(g, c, k):
                for h in range(CH):
                    act.wait_ge(count_ready[h], EB * (UNITS * g + c) + k + 1)
                    nc.scalar.activation(wts[:, h, EB * (c % 2) + k, :], count_ps[h][:], ACT.Relu,
                                         bias=float(BIAS - DROP)).then_inc(wts_ready[h], 1)

            act.wait_ge(w_loaded, 32)
            nc.scalar.activation(w2_abs[:], w2[:], ACT.Abs).then_inc(w_abs_set, 1)
            act.wait_ge(centred, 1)
            nc.scalar.activation(sq[:], cen[:], ACT.Square).then_inc(squared, 1)
            act.wait_ge(var_set, 1)
            nc.scalar.activation(std[:], var[:], ACT.Sqrt).then_inc(std_set, 1)
            for k in range(EB):
                weights(0, 0, k)

            def high_half(q):
                act.wait_ge(support_ready, q + 1)
                nc.scalar.activation(support[:, 8 * q:8 * q + 8, 0, :],
                                     sup_ps(q)[:].rearrange("p (t d) -> p t d", d=D), ACT.Copy).then_inc(high_set, 1)

            def low_half(q):
                act.wait_ge(rest_set, q + 1)
                nc.scalar.activation(support[:, 8 * q:8 * q + 8, 1, :], rest[:, 8 * q:8 * q + 8, :], ACT.Copy,
                                     scale=float(2 ** HALF_BITS)).then_inc(support_set, 1)

            for q in range(4):
                high_half(q)
                if q:
                    low_half(q - 1)
            low_half(3)

            with act.Fori(0, GROUPS - 1) as g:
                for c in range(1, UNITS + 1):
                    for k in range(EB):
                        weights(g, c, k)
            for c in range(1, UNITS):
                for k in range(EB):
                    weights(GROUPS - 1, c, k)

        @block.vector
        def _(dve):
            steps = [0]

            def then_next(ins):
                steps[0] += 1
                ins.then_inc(dve_step, 1)
                dve.wait_ge(dve_step, steps[0])

            def make_mask(g, c, h):
                u = UNITS * g + c
                if not (g is 0 and c < 2):
                    dve.wait_ge(words_ready[h], u - 1)
                wait_apart(dve, load_done[c % RING][h], 16 * ((UNITS // RING) * g + c // RING + 1))
                src = adj_ring[:, c % RING, h].rearrange("p t (e q) -> p t e q", e=EB)
                dst = mask[:, c % 2, h].rearrange("p t (q e) -> p t e q", e=EB)
                nc.vector.tensor_scalar(dst, src, 0.0, None, ALU.not_equal, saturate=False)\
                  .then_inc(mask_ready[h], 1)

            def copy_words(g, c, h):
                u = UNITS * g + c
                dve.wait_ge(words_ready[h], u + 1)
                nc.vector.tensor_copy(mask_t[:, c % 2, h].rearrange("p i e -> p (i e)").bitcast(U32),
                                      words_ps[h][:].bitcast(U32)).then_inc(mask_t_ready[h], 1)

            def results(g):
                for h in range(CH):
                    dve.wait_ge(product_done[h], TILES * (g + 1))
                    nc.vector.tensor_copy(acc_sb[:, h], acc_ps[h][:]).then_inc(acc_copied[h], 1)
                for h in range(CH):
                    dve.wait_ge(rows_ready[h], g + 1)
                    if g is not 0:
                        dve.wait_ge(out_stored[h], 16 * g)
                    rows = rows_ps[h][:, 0:CT * D].rearrange("p (t d) -> p t d", t=CT)
                    t0 = CH * CT * g + CT * h
                    nc.vector.tensor_tensor(out_sb[:, h], rows, x_bias[:, bass.ds(t0, CT), :], ALU.add)\
                      .then_inc(out_ready[h], 1)

            dve.wait_ge(x_loaded, 16)
            then_next(nc.vector.tensor_reduce(row_sum[:], xs[:], AX.X, ALU.add))
            nc.vector.tensor_scalar(mean[:], row_sum[:], 1.0 / D, None, ALU.mult).then_inc(mean_set, 1)
            make_mask(0, 0, 0)
            make_mask(0, 0, 1)
            dve.wait_ge(w_loaded, 32)
            dve.wait_ge(bound_ready, 1)
            then_next(nc.vector.tensor_scalar(bound[:], rows_ps[1][:, 0:P], LN_BOUND_FLOOR, None, ALU.max))
            then_next(nc.vector.tensor_scalar(pow2[:].bitcast(I32), bound[:].bitcast(I32), 0x7F800000, None,
                                              ALU.bitwise_and))
            then_next(nc.vector.reciprocal(inv2[:], pow2[:]))
            nc.vector.scalar_tensor_tensor(out=w2_sc[:], in0=w2[:], scalar=float(2 ** SUP_BITS), in1=inv2[:],
                                           op0=ALU.mult, op1=ALU.mult).then_inc(w_scaled, 1)
            dve.wait_ge(unscale_set, 1)
            nc.vector.tensor_tensor(unscale[:], unscale[:], pow2[:, 0:D], ALU.mult).then_inc(unscale_ready, 1)
            copy_words(0, 0, 0)
            copy_words(0, 0, 1)
            dve.wait_ge(squared, 1)
            then_next(nc.vector.tensor_reduce(sq_sum[:], sq[:], AX.X, ALU.add))
            nc.vector.tensor_scalar(var[:], sq_sum[:], 1.0 / D, EPS, ALU.mult, ALU.add).then_inc(var_set, 1)
            dve.wait_ge(std_set, 1)
            then_next(nc.vector.reciprocal(rstd0[:], std[:]))
            then_next(nc.vector.tensor_tensor(nw1[:], rstd0[:], rstd0[:], ALU.mult))
            dve.wait_ge(var_set, 1)
            then_next(nc.vector.tensor_tensor(nw2[:], nw1[:], var[:], ALU.mult))
            then_next(nc.vector.tensor_scalar(nw3[:], nw2[:], -0.5, 1.5, ALU.mult, ALU.add))
            then_next(nc.vector.tensor_tensor(rstd[:], rstd0[:], nw3[:], ALU.mult))
            dve.wait_ge(centred, 1)
            nc.vector.scalar_tensor_tensor(out=h_sb[:], in0=cen[:], scalar=0.0,
                                           in1=rstd[:].unsqueeze(2).broadcast_to([P, TILES, D]),
                                           op0=ALU.max, op1=ALU.mult).then_inc(h_set, 1)
            make_mask(0, 1, 0)
            make_mask(0, 1, 1)
            for q in range(4):
                dve.wait_ge(h_turned, q + 1)
                nc.vector.tensor_copy(h_t[:, 4 * q:4 * q + 4, :].rearrange("p a b -> p (a b)"), ht_ps(q)[:])\
                  .then_inc(h_t_set, 1)
                if q == 1:
                    for h in range(CH):
                        copy_words(0, 1, h)
                        make_mask(0, 2, h)
            for q in range(4):
                dve.wait_ge(high_set, q + 1)
                nc.vector.tensor_tensor(rest[:, 8 * q:8 * q + 8, :],
                                        sup_ps(q)[:].rearrange("p (t d) -> p t d", d=D),
                                        support[:, 8 * q:8 * q + 8, 0, :], ALU.subtract).then_inc(rest_set, 1)

            def stage(g, c):
                for h in range(CH):
                    if not (g is GROUPS - 1 and c + 2 >= UNITS):
                        make_mask(g, c + 2, h)
                    if not (g is GROUPS - 1 and c + 1 >= UNITS):
                        copy_words(g, c + 1, h)

            dve.wait_ge(x_bias_set, 1)
            for c in range(1, UNITS + 1):
                stage(0, c)
            results(0)
            with dve.Fori(1, GROUPS - 1) as g:
                for c in range(1, UNITS + 1):
                    stage(g, c)
                results(g)
            for c in range(1, UNITS):
                stage(GROUPS - 1, c)
            results(GROUPS - 1)

        @block.tensor
        def _(pe):
            def turn_words(g, c, h):
                pe.wait_ge(mask_ready[h], UNITS * g + c + 1)
                for t in range(CT):
                    ins = nc.tensor.transpose(words_ps[h][:, t * P:(t + 1) * P],
                                              mask[:, c % 2, h, t, :].bitcast(F32), ident[:])
                ins.then_inc(words_ready[h], 1)

            def masks_of(c, h, k):
                return mask_t[:, c % 2, h, :, EB - 1 - k]

            def count(g, c, k, h):
                u = UNITS * g + c
                first = c % UNITS == 0 and k == 0
                if not (g is 0 and c == 0 and first):
                    wait_apart(pe, wts_ready[h], EB * u + k)
                if not first:
                    pc, pk = (c, k - 1) if k else (c - 1, EB - 1)
                    nc.tensor.matmul(count_ps[h][:], to_left[:], masks_of(pc, h, pk), start=False, stop=True,
                                     skip_group_check=True)
                if k == 0:
                    wait_apart(pe, mask_t_ready[h], u + 1)
                nc.tensor.matmul(count_ps[h][:], this_block[:], masks_of(c, h, k), start=first, stop=True,
                                 skip_group_check=True).then_inc(count_ready[h], 1)

            def product(g, c, k, h):
                if c == 0 and k == 0:
                    if g is not 0:
                        pe.wait_ge(acc_copied[h], g)
                pe.wait_ge(wts_ready[h], EB * (UNITS * g + c) + k + 1)
                b = TILES - 1 - EB * c - k
                nc.tensor.matmul(acc_ps[h][:], support[:, b].rearrange("p s d -> p (s d)"),
                                 wts[:, h, EB * (c % 2) + k, :].bitcast(BF16),
                                 start=(c == 0 and k == 0), stop=(c == UNITS - 1 and k == EB - 1))\
                  .then_inc(product_done[h], 1)

            def unit(g, c, turn_next):
                closing = c == UNITS
                for k in range(EB):
                    for h in range(CH):
                        count(g, c, k, h)
                        for kk in ([[0, 1], [2], [3], []][k] if closing else [k]):
                            product(g, c - 1, kk, h)
                    if turn_next and k in (1, 2):
                        turn_words(g, c + 1, k - 1)

            def to_rows(g):
                for h in range(CH):
                    pe.wait_ge(acc_copied[h], g + 1)
                    if g is not 0:
                        pe.wait_ge(out_ready[h], g)
                    for t in range(CT):
                        ins = nc.tensor.matmul(rows_ps[h][:, t * D:(t + 1) * D], acc_sb[:, h, t * P:(t + 1) * P], unscale[:],
                                               start=True, stop=True, skip_group_check=True)
                    ins.then_inc(rows_ready[h], 1)

            pe.wait_ge(ident_set, 1)
            turn_words(0, 0, 0)
            turn_words(0, 0, 1)
            pe.wait_ge(ones_set, 1)
            pe.wait_ge(w_abs_set, 1)
            nc.tensor.matmul(rows_ps[1][:, 0:P], ones[:], w2_abs[:], start=True, stop=True).then_inc(bound_ready, 1)
            pe.wait_ge(count_mats_set, 1)
            for k in range(EB):
                for h in range(CH):
                    count(0, 0, k, h)
            pe.wait_ge(h_set, 1)
            for q in range(4):
                if q == 2:
                    for h in range(CH):
                        turn_words(0, 1, h)
                if q >= 2:
                    pe.wait_ge(h_t_set, q - 1)
                for a in range(4):
                    pair = h_sb[:, 8 * q + 2 * a:8 * q + 2 * a + 2, :].rearrange("p t d -> p (t d)")
                    ins = nc.tensor.transpose(ht_ps(q)[:, a * P:(a + 1) * P], pair, ident[:])
                ins.then_inc(h_turned, 1)
            pe.wait_ge(w_scaled, 1)
            for q in range(4):
                pe.wait_ge(h_t_set, q + 1)
                if q >= 2:
                    pe.wait_ge(rest_set, q - 1)
                for a in range(4):
                    ins = nc.tensor.matmul(sup_ps(q)[:, a * P:(a + 1) * P], h_t[:, 4 * q + a, :], w2_sc[:],
                                           start=True, stop=True, skip_group_check=True)
                ins.then_inc(support_ready, 1)
            pe.wait_ge(support_set, 4)
            pe.wait_ge(unscale_ready, 1)
            for h in range(CH):
                pe.wait_ge(h_t_set, 4)

            def group(g):
                for c in range(1, UNITS):
                    unit(g, c, not (g is GROUPS - 1 and c == UNITS - 1))
                if g is not GROUPS - 1:
                    unit(g, UNITS, True)
                else:
                    for k in range(EB):
                        for h in range(CH):
                            product(g, UNITS - 1, k, h)
                to_rows(g)

            group(0)
            with pe.Fori(1, GROUPS - 1) as g:
                group(g)
            group(GROUPS - 1)


def kernel(x, adj, L0_gnn_weight, L0_gnn_bias):
    import numpy as np
    import concourse.bacc as bacc
    from concourse.bass_utils import run_bass_kernel_spmd

    nc = bacc.Bacc("TRN2", target_bir_lowering=False, num_devices=1)
    ins = {"x": x, "adj": adj, "weight": L0_gnn_weight, "bias": L0_gnn_bias}
    arrays = {f"in_{n}": np.ascontiguousarray(a) for n, a in ins.items()}
    args = [nc.dram_tensor(n, a.shape, mybir.dt.from_np(a.dtype), kind="ExternalInput").ap()
            for n, a in arrays.items()]
    out = nc.dram_tensor("out", x.shape, F32, kind="ExternalOutput").ap()
    neighbour_decay_kernel(nc, *args, out)
    r = run_bass_kernel_spmd(nc, [arrays], core_ids=[0])
    return r.results[0]["out"]
```

```python
from contextlib import ExitStack

import concourse.bass as bass
from concourse import mybir

ALU = mybir.AluOpType
ACT = mybir.ActivationFunctionType
AX = mybir.AxisListType
F32 = mybir.dt.float32
F16 = mybir.dt.float16
BF16 = mybir.dt.bfloat16
FP8 = mybir.dt.float8e4
I16 = mybir.dt.int16
I32 = mybir.dt.int32
U32 = mybir.dt.uint32

P = 128
MAX_NEIGH = 100
EXP_ONE = 128
BF16_BIAS = 127
BIAS = MAX_NEIGH * EXP_ONE
SET = 2.0
BYTES_BIT = 0x40404040
DROP = 16384
EPS = 1e-5
HALF_BITS = 11
SUP_BITS = 10
OUT_BITS = BF16_BIAS - MAX_NEIGH
LN_BOUND_FLOOR = 2.0 ** -100


def neighbour_decay_kernel(nc, x, adj, weight, bias, out):
    N, D = x.shape
    TILES = N // P
    CH = 2
    CT = 4
    ROWS = CT * P
    EB = 4
    COLS = EB * P
    UNITS = N // COLS
    GROUPS = N // (CH * ROWS)
    RING = 4
    QT = 8
    QUARTS = TILES // QT
    assert D == 64 and TILES == 32 and UNITS == 8 and UNITS % RING == 0

    adj_v = adj.rearrange("(g h t p) j -> g h p t j", h=CH, t=CT, p=P)
    x_v = x.rearrange("(s p t) d -> p s t d", p=P, t=CT)
    out_v = out.rearrange("(g h p t) d -> g h p t d", h=CH, t=CT, p=P)
    bias_v = bias.rearrange("(a d) -> a d", a=1)

    with ExitStack() as ctx:
        def sb(name, shape, dt):
            return ctx.enter_context(nc.sbuf_tensor(name, shape, dt))

        def psum(name):
            return ctx.enter_context(nc.psum_tensor(name, [P, 512], F32))

        def sem(name):
            return ctx.enter_context(nc.semaphore(name))

        adj_ring = sb("adj_ring", [P, RING, CH, CT, COLS], F32)
        mask = sb("mask", [P, 2, CH, CT, COLS], FP8)
        pairs = sb("pairs", [P, CH, CT // 2, P], U32)
        packed = sb("packed", [P, 2, CH, P], U32)
        mask_t = sb("mask_t", [P, 2, CH, ROWS, EB], FP8)
        wts = sb("wts", [P, CH, 2 * EB, ROWS], I16)
        acc_sb = sb("acc_sb", [P, CH, ROWS], F32)
        ident = sb("ident", [P, P], F32)
        ones = sb("ones", [P, P], F32)
        this_block = sb("this_block", [P, P], BF16)
        to_left = sb("to_left", [P, P], BF16)
        unscale = sb("unscale", [P, D], F32)
        xs = sb("xs", [P, TILES, D], F32)
        bias_sb = sb("bias_sb", [P, D], F32)
        out_sb = sb("out_sb", [P, TILES, D], F32)
        cen = sb("cen", [P, TILES, D], F32)
        sq = sb("sq", [P, TILES, D], F32)
        row_sum = sb("row_sum", [P, TILES], F32)
        mean = sb("mean", [P, TILES], F32)
        sq_sum = sb("sq_sum", [P, TILES], F32)
        var = sb("var", [P, TILES], F32)
        std = sb("std", [P, TILES], F32)
        rstd0 = sb("rstd0", [P, TILES], F32)
        nw1 = sb("nw1", [P, TILES], F32)
        nw2 = sb("nw2", [P, TILES], F32)
        nw3 = sb("nw3", [P, TILES], F32)
        rstd = sb("rstd", [P, TILES], F32)
        h_sb = sb("h_sb", [P, TILES, D], F32)
        h_t = sb("h_t", [D, TILES * P], F32)
        w_sb = sb("w_sb", [D, D], F32)
        w_abs = sb("w_abs", [D, D], F32)
        w_sc = sb("w_sc", [D, D], F32)
        bound = sb("bound", [P, D], F32)
        pow2 = sb("pow2", [P, D], F32)
        inv2 = sb("inv2", [D, D], F32)
        rest = sb("rest", [P, TILES, D], F32)
        support = sb("support", [P, TILES, 2, D], F16)

        words_ps = [psum(f"words_ps{i}") for i in range(2)]
        count_ps = [psum(f"count_ps{h}") for h in range(CH)]
        acc_ps = [psum(f"acc_ps{h}") for h in range(CH)]
        rows_ps = [psum(f"rows_ps{h}") for h in range(CH)]

        load_done = [[sem(f"load_done{r}_{h}") for h in range(CH)] for r in range(RING)]
        x_loaded = [sem(f"x_loaded{n}") for n in range(QUARTS)]
        w_loaded = sem("w_loaded")
        bias_loaded = sem("bias_loaded")
        pool_step = sem("pool_step")
        ident_set = sem("ident_set")
        count_mats_set = sem("count_mats_set")
        unscale_set = sem("unscale_set")
        ones_set = sem("ones_set")
        out_begun = sem("out_begun")
        mean_set = sem("mean_set")
        centred = sem("centred")
        squared = sem("squared")
        var_set = sem("var_set")
        std_set = sem("std_set")
        rstd0_set = sem("rstd0_set")
        h_set = sem("h_set")
        w_abs_set = sem("w_abs_set")
        bound_ready = sem("bound_ready")
        w_scaled = sem("w_scaled")
        unscale_ready = sem("unscale_ready")
        h_turned = sem("h_turned")
        h_t_set = sem("h_t_set")
        support_ready = sem("support_ready")
        high_set = sem("high_set")
        rest_set = sem("rest_set")
        support_set = sem("support_set")
        dve_step = sem("dve_step")
        mask_ready = [sem(f"mask_ready{h}") for h in range(CH)]
        pairs_ready = sem("pairs_ready")
        packed_ready = sem("packed_ready")
        words_ready = sem("words_ready")
        mask_t_ready = sem("mask_t_ready")
        count_ready = [sem(f"count_ready{h}") for h in range(CH)]
        wts_ready = [sem(f"wts_ready{h}") for h in range(CH)]
        product_done = [sem(f"product_done{h}") for h in range(CH)]
        acc_copied = [sem(f"acc_copied{h}") for h in range(CH)]
        rows_ready = [sem(f"rows_ready{h}") for h in range(CH)]
        out_ready = [sem(f"out_ready{h}") for h in range(CH)]
        last_stored = [sem(f"last_stored{h}") for h in range(CH)]
        out_stored = [sem(f"out_stored{h}") for h in range(CH)]

        def wait_apart(eng, s, value):
            eng.wait_ge(s, value)
            if not isinstance(value, int):
                eng.sem_inc(waits_carried, 1)

        def quart(t, n):
            return t[:, QT * (QUARTS - 1 - n):QT * (QUARTS - n)]

        waits_carried = sem("waits_carried")

        block = ctx.enter_context(nc.Block())

        @block.sync
        def _(sp):
            def load(g, c, again):
                for h in range(CH):
                    if again:
                        wait_apart(sp, mask_ready[h], UNITS * g + c - RING + 1)
                    j0 = N - COLS * (c + 1)
                    sp.dma_start(adj_ring[:, c % RING, h], adj_v[g, h, :, :, j0:j0 + COLS])\
                      .then_inc(load_done[c % RING][h], 16)

            def load_x(n):
                t0 = QT * (QUARTS - 1 - n)
                sp.dma_start(xs[:, t0:t0 + QT].rearrange("p (s t) d -> p s t d", t=CT),
                             x_v[:, t0 // CT:(t0 + QT) // CT]).then_inc(x_loaded[n], 16)

            for c in range(UNITS):
                if c == 0:
                    load_x(0)
                load(0, c, c >= RING)
                if 1 <= c < QUARTS:
                    load_x(c)
            sp.dma_start(bias_sb[:], bias_v.broadcast_to([P, D])).then_inc(bias_loaded, 16)
            with sp.Fori(1, GROUPS) as g:
                for c in range(UNITS):
                    load(g, c, True)
            for h in range(CH):
                sp.wait_ge(out_ready[h], GROUPS)
                t0 = CH * CT * (GROUPS - 1) + CT * h
                sp.dma_start(out_v[GROUPS - 1, h], out_sb[:, t0:t0 + CT]).then_inc(last_stored[h], 16)
            for h in range(CH):
                sp.wait_ge(last_stored[h], 16)

        @block.gpsimd
        def _(pool):
            steps = [0]

            def then_next(ins):
                steps[0] += 1
                ins.then_inc(pool_step, 1)
                pool.wait_ge(pool_step, steps[0])

            def fill_where(t, keep, base, step, cm, fill):
                return nc.gpsimd.affine_select(out=t, in_=t, compare_op=keep, fill=fill, base=base,
                                               pattern=[[step, t.shape[1]]], channel_multiplier=cm)

            then_next(nc.gpsimd.memset(ident[:], 0.0))
            fill_where(ident[:], ALU.not_equal, 0, -1, 1, 1.0).then_inc(ident_set, 1)
            then_next(nc.gpsimd.memset(this_block[:], 0.0))
            then_next(fill_where(this_block[:], ALU.is_ge, 0, 1, -1, -EXP_ONE / SET))
            then_next(fill_where(this_block[:], ALU.not_equal, 0, 1, -1, DROP / SET))
            then_next(nc.gpsimd.memset(to_left[:], -EXP_ONE / SET))
            then_next(fill_where(to_left[:], ALU.is_ge, 0, 1, -1, 0.0))
            fill_where(to_left[:], ALU.not_equal, 0, 1, -1, -(EXP_ONE + DROP) / SET).then_inc(count_mats_set, 1)
            nc.gpsimd.memset(ones[:], 1.0).then_inc(ones_set, 1)
            then_next(nc.gpsimd.memset(unscale[:], 0.0))
            then_next(fill_where(unscale[:], ALU.not_equal, 0, -1, 1, 2.0 ** (OUT_BITS - SUP_BITS)))
            fill_where(unscale[:], ALU.not_equal, -D, -1, 1,
                       2.0 ** (OUT_BITS - SUP_BITS - HALF_BITS)).then_inc(unscale_set, 1)
            def centre(n):
                pool.wait_ge(x_loaded[n], 16)
                pool.wait_ge(mean_set, n + 1)
                nc.gpsimd.tensor_tensor(quart(cen, n), quart(xs, n),
                                        quart(mean, n).unsqueeze(2).broadcast_to([P, QT, D]),
                                        ALU.subtract).then_inc(centred, 1)

            def normalise(n):
                pool.wait_ge(rstd0_set, n + 1)
                then_next(nc.gpsimd.tensor_tensor(quart(nw1, n), quart(rstd0, n), quart(rstd0, n), ALU.mult))
                pool.wait_ge(var_set, n + 1)
                then_next(nc.gpsimd.tensor_tensor(quart(nw2, n), quart(nw1, n), quart(var, n), ALU.mult))
                then_next(nc.gpsimd.tensor_scalar(quart(nw3, n), quart(nw2, n), -0.5, 1.5, ALU.mult, ALU.add))
                then_next(nc.gpsimd.tensor_tensor(quart(rstd, n), quart(rstd0, n), quart(nw3, n), ALU.mult))
                nc.gpsimd.tensor_tensor(quart(h_sb, n), quart(cen, n),
                                        quart(rstd, n).unsqueeze(2).broadcast_to([P, QT, D]),
                                        ALU.mult).then_inc(h_set, 1)

            for n in range(QUARTS):
                centre(n)
                normalise(n)
            pool.wait_ge(bias_loaded, 16)
            nc.gpsimd.tensor_tensor(out_sb[:], xs[:], bias_sb[:].unsqueeze(1).broadcast_to([P, TILES, D]),
                                    ALU.add).then_inc(out_begun, 1)
            for g in range(GROUPS - 1):
                for h in range(CH):
                    pool.wait_ge(out_ready[h], g + 1)
                    t0 = CH * CT * g + CT * h
                    pool.dma_start(out_v[g, h], out_sb[:, t0:t0 + CT]).then_inc(out_stored[h], 16)
            for h in range(CH):
                pool.wait_ge(out_stored[h], 16 * (GROUPS - 1))

        @block.scalar
        def _(act):
            def weights(g, c, k):
                for h in range(CH):
                    act.wait_ge(count_ready[h], EB * (UNITS * g + c) + k + 1)
                    nc.scalar.activation(wts[:, h, EB * (c % 2) + k, :], count_ps[h][:], ACT.Relu,
                                         bias=float(BIAS - DROP)).then_inc(wts_ready[h], 1)

            def square(n):
                act.wait_ge(centred, n + 1)
                nc.scalar.activation(quart(sq, n), quart(cen, n), ACT.Square).then_inc(squared, 1)

            def root(n):
                act.wait_ge(var_set, n + 1)
                nc.scalar.activation(quart(std, n), quart(var, n), ACT.Sqrt).then_inc(std_set, 1)

            def copy_h_t(n):
                act.wait_ge(h_turned, n + 1)
                c0 = P * QT * (QUARTS - 1 - n)
                dst = h_t[:, c0:c0 + P * QT].rearrange("d (s p a b) -> d b s a p", s=QT // CT, p=P, a=2)
                for b in range(2):
                    src = rows_ps[0][b * D:(b + 1) * D, :].rearrange("d (s a p) -> d s a p", s=QT // CT, a=2)
                    nc.scalar.activation(dst[:, b], src, ACT.Relu).then_inc(h_t_set, 1)

            def high_half(n):
                act.wait_ge(support_ready, n + 1)
                nc.scalar.activation(quart(support, n)[:, :, 0, :], rows_ps[1][:].rearrange("p (t d) -> p t d", d=D),
                                     ACT.Copy).then_inc(high_set, 1)

            def low_half(n):
                act.wait_ge(rest_set, n + 1)
                nc.scalar.activation(quart(support, n)[:, :, 1, :], quart(rest, n), ACT.Copy,
                                     scale=float(2 ** HALF_BITS)).then_inc(support_set, 1)

            act.dma_start(w_sb[:], weight).then_inc(w_loaded, 16)
            act.preload_act_table(ACT.Sqrt)
            act.wait_ge(w_loaded, 16)
            nc.scalar.activation(w_abs[:], w_sb[:], ACT.Abs).then_inc(w_abs_set, 1)
            square(0)
            root(0)
            copy_h_t(0)
            for c in range(UNITS + 1):
                new, turned, made = (c + 2) // 2, (c + 1) // 2, c // 2
                for k in range(EB):
                    weights(0, c, k)
                    if c % 2 and turned < QUARTS and k == 3:
                        copy_h_t(turned)
                    if 0 < c and c % 2 == 0 and new < QUARTS and k in (1, 2):
                        (square, root)[k - 1](new)
                    if c == 1 and k in (0, 1):
                        (square, root)[k](1)
                    if c % 2 == 0 and made < QUARTS and k == 0:
                        high_half(made)
                    if c % 2 == 0 and made < QUARTS and k == (2 if c else 3):
                        low_half(made)
            with act.Fori(1, GROUPS - 1) as g:
                for c in range(1, UNITS + 1):
                    for k in range(EB):
                        weights(g, c, k)
            for c in range(1, UNITS):
                for k in range(EB):
                    weights(GROUPS - 1, c, k)
            act.wait_ge(rows_ready[1], GROUPS - 1)
            act.wait_ge(product_done[1], TILES * GROUPS)
            nc.scalar.activation(acc_sb[:, 1], acc_ps[1][:], ACT.Copy).then_inc(acc_copied[1], 1)

        @block.vector
        def _(dve):
            steps = [0]

            def then_next(ins):
                steps[0] += 1
                ins.then_inc(dve_step, 1)
                dve.wait_ge(dve_step, steps[0])

            def make_mask(g, c, h):
                wait_apart(dve, load_done[c % RING][h], 16 * ((UNITS // RING) * g + c // RING + 1))
                src = adj_ring[:, c % RING, h].rearrange("p t (e q) -> p t e q", e=EB)
                dst = mask[:, c % 2, h].rearrange("p t (q e) -> p t e q", e=EB)
                nc.vector.tensor_scalar(dst, src, 0.0, SET, ALU.not_equal, ALU.mult, saturate=False)\
                  .then_inc(mask_ready[h], 1)

            def pack(g, c):
                u = UNITS * g + c
                for h in range(CH):
                    dve.wait_ge(mask_ready[h], u + 1)
                if not (g is 0 and c < 2):
                    dve.wait_ge(words_ready, u - 1)
                tiles = mask[:, c % 2].rearrange("p h (a b) n -> p (h a) b n", b=2).bitcast(U32)
                nc.vector.scalar_tensor_tensor(out=pairs[:].rearrange("p h a q -> p (h a) q"),
                                               in0=tiles[:, :, 1], scalar=1, in1=tiles[:, :, 0],
                                               op0=ALU.logical_shift_right, op1=ALU.bitwise_or)\
                  .then_inc(pairs_ready, 1)
                dve.wait_ge(pairs_ready, u + 1)
                nc.vector.scalar_tensor_tensor(out=packed[:, c % 2], in0=pairs[:, :, 1], scalar=2,
                                               in1=pairs[:, :, 0], op0=ALU.logical_shift_right,
                                               op1=ALU.bitwise_or).then_inc(packed_ready, 1)

            def unpack(g, c):
                dve.wait_ge(words_ready, UNITS * g + c + 1)
                words = words_ps[c % 2][:, 0:CH * P].bitcast(U32).rearrange("p (h i) -> p h i", i=P)
                tiles = mask_t[:, c % 2].rearrange("p h (t i) e -> p h t (i e)", t=CT).bitcast(U32)
                for t in range(CT):
                    ins = nc.vector.tensor_scalar(tiles[:, :, t], words, t, BYTES_BIT, ALU.logical_shift_left,
                                                  ALU.bitwise_and)
                ins.then_inc(mask_t_ready, 1)

            def copy_sums(g, chains):
                for h in chains:
                    dve.wait_ge(product_done[h], TILES * (g + 1))
                    nc.vector.tensor_copy(acc_sb[:, h], acc_ps[h][:]).then_inc(acc_copied[h], 1)

            def add_rows(g):
                for h in range(CH):
                    dve.wait_ge(rows_ready[h], g + 1)
                    rows = rows_ps[h][:, 0:CT * D].rearrange("p (t d) -> p t d", t=CT)
                    place = out_sb[:, bass.ds(CH * CT * g + CT * h, CT), :]
                    nc.vector.tensor_tensor(place, rows, place, ALU.add).then_inc(out_ready[h], 1)

            def means(n):
                dve.wait_ge(x_loaded[n], 16)
                then_next(nc.vector.tensor_reduce(quart(row_sum, n), quart(xs, n), AX.X, ALU.add))
                nc.vector.tensor_scalar(quart(mean, n), quart(row_sum, n), 1.0 / D, None, ALU.mult)\
                  .then_inc(mean_set, 1)

            def variances(n):
                dve.wait_ge(squared, n + 1)
                then_next(nc.vector.tensor_reduce(quart(sq_sum, n), quart(sq, n), AX.X, ALU.add))
                nc.vector.tensor_scalar(quart(var, n), quart(sq_sum, n), 1.0 / D, EPS, ALU.mult, ALU.add)\
                  .then_inc(var_set, 1)

            def reciprocals(n):
                dve.wait_ge(std_set, n + 1)
                nc.vector.reciprocal(quart(rstd0, n), quart(std, n)).then_inc(rstd0_set, 1)

            def leave_rest(n):
                dve.wait_ge(high_set, n + 1)
                nc.vector.tensor_tensor(quart(rest, n), rows_ps[1][:].rearrange("p (t d) -> p t d", d=D),
                                        quart(support, n)[:, :, 0, :], ALU.subtract).then_inc(rest_set, 1)

            def scales():
                dve.wait_ge(w_loaded, 16)
                dve.wait_ge(bound_ready, 1)
                then_next(nc.vector.tensor_scalar(bound[:], rows_ps[1][:, 0:D], LN_BOUND_FLOOR, None, ALU.max))
                then_next(nc.vector.tensor_scalar(pow2[:].bitcast(I32), bound[:].bitcast(I32), 0x7F800000, None,
                                                  ALU.bitwise_and))
                then_next(nc.vector.reciprocal(inv2[:], pow2[0:D]))
                nc.vector.scalar_tensor_tensor(out=w_sc[:], in0=w_sb[:], scalar=float(2 ** SUP_BITS), in1=inv2[:],
                                               op0=ALU.mult, op1=ALU.mult).then_inc(w_scaled, 1)
                dve.wait_ge(unscale_set, 1)
                nc.vector.tensor_tensor(unscale[:], unscale[:], pow2[:], ALU.mult).then_inc(unscale_ready, 1)

            def stage(g, c, first=False):
                new, made = (c + 2) // 2, c // 2
                entering = first and c % 2 == 0 and new < QUARTS
                last = g is GROUPS - 1
                if entering:
                    means(new)
                if not (last and c + 2 >= UNITS):
                    make_mask(g, c + 2, 0)
                if first and c % 2 == 0 and 0 < made < QUARTS:
                    leave_rest(made)
                if entering:
                    variances(new)
                if not (last and c + 1 >= UNITS):
                    unpack(g, c + 1)
                if entering:
                    reciprocals(new)
                if c == UNITS:
                    copy_sums(g, range(CH))
                if not (last and c + 2 >= UNITS):
                    make_mask(g, c + 2, 1)
                    pack(g, c + 2)
                if c == 1 and not first:
                    add_rows(g - 1)

            means(0)
            scales()
            make_mask(0, 0, 0)
            variances(0)
            reciprocals(0)
            make_mask(0, 0, 1)
            pack(0, 0)
            unpack(0, 0)
            for h in range(CH):
                make_mask(0, 1, h)
            pack(0, 1)
            leave_rest(0)
            unpack(0, 1)
            means(1)
            for h in range(CH):
                make_mask(0, 2, h)
            pack(0, 2)
            variances(1)
            reciprocals(1)
            for c in range(1, UNITS):
                stage(0, c, True)
            dve.wait_ge(out_begun, 1)
            stage(0, UNITS, True)
            with dve.Fori(1, GROUPS - 1) as g:
                for c in range(1, UNITS + 1):
                    stage(g, c)
            for c in range(1, UNITS):
                stage(GROUPS - 1, c)
            copy_sums(GROUPS - 1, [0])
            add_rows(GROUPS - 1)

        @block.tensor
        def _(pe):
            def turn_words(g, c):
                pe.wait_ge(packed_ready, UNITS * g + c + 1)
                for h in range(CH):
                    ins = nc.tensor.transpose(words_ps[c % 2][:, h * P:(h + 1) * P],
                                              packed[:, c % 2, h].bitcast(F32), ident[:])
                ins.then_inc(words_ready, 1)

            def masks_of(c, h, k):
                return mask_t[:, c % 2, h, :, EB - 1 - k]

            def count(g, c, k, h):
                u = UNITS * g + c
                first = c % UNITS == 0 and k == 0
                if not (g is 0 and c == 0 and first):
                    wait_apart(pe, wts_ready[h], EB * u + k)
                if not first:
                    pc, pk = (c, k - 1) if k else (c - 1, EB - 1)
                    nc.tensor.matmul(count_ps[h][:], to_left[:], masks_of(pc, h, pk), start=False, stop=True,
                                     skip_group_check=True)
                if k == 0 and h == 0:
                    wait_apart(pe, mask_t_ready, u + 1)
                nc.tensor.matmul(count_ps[h][:], this_block[:], masks_of(c, h, k), start=first, stop=True,
                                 skip_group_check=True).then_inc(count_ready[h], 1)

            def product(g, c, k, h):
                if c == 0 and k == 0:
                    if g is not 0:
                        pe.wait_ge(acc_copied[h], g)
                pe.wait_ge(wts_ready[h], EB * (UNITS * g + c) + k + 1)
                if g is 0 and c % 2 == 0 and k == 0:
                    pe.wait_ge(support_set, c // 2 + 1)
                b = TILES - 1 - EB * c - k
                nc.tensor.matmul(acc_ps[h][:], support[:, b].rearrange("p s d -> p (s d)"),
                                 wts[:, h, EB * (c % 2) + k, :].bitcast(BF16),
                                 start=(c == 0 and k == 0), stop=(c == UNITS - 1 and k == EB - 1))\
                  .then_inc(product_done[h], 1)

            def turn_h(n):
                if n:
                    pe.wait_ge(h_t_set, 2 * n)
                pe.wait_ge(h_set, n + 1)
                for a in range(QT // 2):
                    t = QT * (QUARTS - 1 - n) + 2 * a
                    ins = nc.tensor.transpose(rows_ps[0][:, a * P:(a + 1) * P],
                                              h_sb[:, t:t + 2, :].rearrange("p t d -> p (t d)"), ident[:])
                ins.then_inc(h_turned, 1)

            def make_support(n):
                if n == 0:
                    pe.wait_ge(w_scaled, 1)
                else:
                    pe.wait_ge(rest_set, n)
                pe.wait_ge(h_t_set, 2 * (n + 1))
                for a in range(QT):
                    j = P * (QT * (QUARTS - 1 - n) + a)
                    ins = nc.tensor.matmul(rows_ps[1][:, a * D:(a + 1) * D], h_t[:, j:j + P], w_sc[:],
                                           start=True, stop=True, skip_group_check=True)
                ins.then_inc(support_ready, 1)

            def unit(g, c, first=False):
                closing = c == UNITS
                turned = (c + 1) // 2
                for k in range(EB):
                    for h in range(CH):
                        count(g, c, k, h)
                        for kk in ([[0, 1], [2], [3], []][k] if closing else [k]) if c else []:
                            product(g, c - 1, kk, h)
                    if k == 1 and not (g is GROUPS - 1 and c == UNITS - 1):
                        turn_words(g, c + 1)
                    if k == 1 and c == 1 and not first:
                        to_rows(g - 1)
                    if first and c % 2 == 0 and c // 2 < QUARTS and k == 0:
                        make_support(c // 2)
                    if first and c % 2 and turned < QUARTS and k == 3:
                        turn_h(turned)

            def to_rows(g):
                for h in range(CH):
                    pe.wait_ge(acc_copied[h], g + 1)
                    for t in range(CT):
                        ins = nc.tensor.matmul(rows_ps[h][:, t * D:(t + 1) * D], acc_sb[:, h, t:ROWS:CT], unscale[:],
                                               start=True, stop=True, skip_group_check=True)
                    ins.then_inc(rows_ready[h], 1)

            pe.wait_ge(ident_set, 1)
            pe.wait_ge(ones_set, 1)
            pe.wait_ge(w_abs_set, 1)
            nc.tensor.matmul(rows_ps[1][:, 0:D], ones[0:D, :], w_abs[:], start=True, stop=True)\
              .then_inc(bound_ready, 1)
            pe.wait_ge(count_mats_set, 1)
            def warm_up(products):
                for _ in range(products):
                    nc.tensor.matmul(count_ps[0][:], to_left[:], to_left[:].unsqueeze(1).broadcast_to([P, 4, P]),
                                     start=True, stop=True, skip_group_check=True)

            warm_up(15)
            turn_words(0, 0)
            turn_h(0)
            warm_up(5)
            for c in range(UNITS):
                unit(0, c, first=True)
            pe.wait_ge(unscale_ready, 1)
            unit(0, UNITS, first=True)
            with pe.Fori(1, GROUPS - 1) as g:
                for c in range(1, UNITS + 1):
                    unit(g, c)
            for c in range(1, UNITS):
                unit(GROUPS - 1, c)
            for h in range(CH):
                for k in range(EB):
                    product(GROUPS - 1, UNITS - 1, k, h)
            to_rows(GROUPS - 1)


def kernel(x, adj, L0_gnn_weight, L0_gnn_bias):
    import numpy as np
    import concourse.bacc as bacc
    from concourse.bass_utils import run_bass_kernel_spmd

    nc = bacc.Bacc("TRN2", target_bir_lowering=False, num_devices=1)
    ins = {"x": x, "adj": adj, "weight": L0_gnn_weight, "bias": L0_gnn_bias}
    arrays = {f"in_{n}": np.ascontiguousarray(a) for n, a in ins.items()}
    args = [nc.dram_tensor(n, a.shape, mybir.dt.from_np(a.dtype), kind="ExternalInput").ap()
            for n, a in arrays.items()]
    out = nc.dram_tensor("out", x.shape, F32, kind="ExternalOutput").ap()
    neighbour_decay_kernel(nc, *args, out)
    r = run_bass_kernel_spmd(nc, [arrays], core_ids=[0])
    return r.results[0]["out"]
```

```python
from contextlib import ExitStack

import concourse.bass as bass
from concourse import mybir

ALU = mybir.AluOpType
ACT = mybir.ActivationFunctionType
AX = mybir.AxisListType
F32 = mybir.dt.float32
F16 = mybir.dt.float16
BF16 = mybir.dt.bfloat16
FP8 = mybir.dt.float8e4
I16 = mybir.dt.int16
U32 = mybir.dt.uint32

P = 128
MAX_NEIGH = 100
EXP_ONE = 128
BF16_BIAS = 127
BIAS = MAX_NEIGH * EXP_ONE
SET = 2.0
BYTES_BIT = 0x40404040
DROP = 16384
EPS = 1e-5
HALF_BITS = 11
H_BITS = 12
OUT_BITS = BF16_BIAS - MAX_NEIGH


def neighbour_decay_kernel(nc, x, adj, weight, bias, out):
    N, D = x.shape
    TILES = N // P
    CH = 2
    CT = 4
    ROWS = CT * P
    EB = 4
    COLS = EB * P
    UNITS = N // COLS
    GROUPS = N // (CH * ROWS)
    RING = 4
    QT = 8
    QUARTS = TILES // QT
    assert D == 64 and TILES == 32 and UNITS == 8 and UNITS % RING == 0

    adj_v = adj.rearrange("(g h t p) j -> g h p t j", h=CH, t=CT, p=P)
    x_v = x.rearrange("(s p t) d -> p s t d", p=P, t=CT)
    out_v = out.rearrange("(g h p t) d -> g h p t d", h=CH, t=CT, p=P)
    bias_v = bias.rearrange("(a d) -> a d", a=1)

    with ExitStack() as ctx:
        def sb(name, shape, dt):
            return ctx.enter_context(nc.sbuf_tensor(name, shape, dt))

        def psum(name):
            return ctx.enter_context(nc.psum_tensor(name, [P, 512], F32))

        def sem(name):
            return ctx.enter_context(nc.semaphore(name))

        adj_ring = sb("adj_ring", [P, RING, CH, CT, COLS], F32)
        mask = sb("mask", [P, 2, CH, CT, COLS], FP8)
        pairs = sb("pairs", [P, CH, CT // 2, P], U32)
        packed = sb("packed", [P, 2, CH, P], U32)
        mask_t = sb("mask_t", [P, 2, CH, ROWS, EB], FP8)
        wts = sb("wts", [P, CH, 2 * EB, ROWS], I16)
        acc_sb = sb("acc_sb", [P, CH, ROWS], F32)
        ident = sb("ident", [P, P], F32)
        ident16 = sb("ident16", [P, P], F16)
        this_block = sb("this_block", [P, P], BF16)
        to_left = sb("to_left", [P, P], BF16)
        w_out = sb("w_out", [P, D], F32)
        xs = sb("xs", [P, TILES, D], F32)
        bias_sb = sb("bias_sb", [P, D], F32)
        out_sb = sb("out_sb", [P, TILES, D], F32)
        cen = sb("cen", [P, TILES, D], F32)
        sq = sb("sq", [P, TILES, D], F32)
        row_sum = sb("row_sum", [P, TILES], F32)
        mean = sb("mean", [P, TILES], F32)
        sq_sum = sb("sq_sum", [P, TILES], F32)
        var = sb("var", [P, TILES], F32)
        std = sb("std", [P, TILES], F32)
        rstd0 = sb("rstd0", [P, TILES], F32)
        nw1 = sb("nw1", [P, TILES], F32)
        nw2 = sb("nw2", [P, TILES], F32)
        nw3 = sb("nw3", [P, TILES], F32)
        rstd = sb("rstd", [P, TILES], F32)
        h_sb = sb("h_sb", [P, TILES, D], F32)
        rest = sb("rest", [P, TILES, D], F32)
        halves = sb("halves", [P, TILES, 2, D], F16)
        h_t = sb("h_t", [2 * D, TILES * P], F16)
        h_rows = sb("h_rows", [P, TILES, 2, D], F16)

        words_ps = [psum(f"words_ps{i}") for i in range(2)]
        count_ps = [psum(f"count_ps{h}") for h in range(CH)]
        acc_ps = [psum(f"acc_ps{h}") for h in range(CH)]
        rows_ps = [psum(f"rows_ps{h}") for h in range(CH)]

        waits_carried = sem("waits_carried")
        load_done = [[sem(f"load_done{r}_{h}") for h in range(CH)] for r in range(RING)]
        x_loaded = [sem(f"x_loaded{n}") for n in range(QUARTS)]
        w_loaded = sem("w_loaded")
        bias_loaded = sem("bias_loaded")
        pool_step = sem("pool_step")
        ident_set = sem("ident_set")
        ident16_set = sem("ident16_set")
        count_mats_set = sem("count_mats_set")
        out_begun = sem("out_begun")
        mean_set = sem("mean_set")
        centred = sem("centred")
        squared = sem("squared")
        var_set = sem("var_set")
        std_set = sem("std_set")
        rstd0_set = sem("rstd0_set")
        h_set = sem("h_set")
        high_set = sem("high_set")
        rest_set = sem("rest_set")
        halves_set = sem("halves_set")
        h_turned = sem("h_turned")
        h_t_set = sem("h_t_set")
        h_back = sem("h_back")
        h_rows_set = sem("h_rows_set")
        w_out_set = sem("w_out_set")
        dve_step = sem("dve_step")
        mask_ready = [sem(f"mask_ready{h}") for h in range(CH)]
        pairs_ready = sem("pairs_ready")
        packed_ready = sem("packed_ready")
        words_ready = sem("words_ready")
        mask_t_ready = sem("mask_t_ready")
        count_ready = [sem(f"count_ready{h}") for h in range(CH)]
        wts_ready = [sem(f"wts_ready{h}") for h in range(CH)]
        product_done = [sem(f"product_done{h}") for h in range(CH)]
        acc_copied = [sem(f"acc_copied{h}") for h in range(CH)]
        rows_ready = [sem(f"rows_ready{h}") for h in range(CH)]
        out_ready = [sem(f"out_ready{h}") for h in range(CH)]
        last_stored = [sem(f"last_stored{h}") for h in range(CH)]
        out_stored = [sem(f"out_stored{h}") for h in range(CH)]

        def wait_apart(eng, s, value):
            eng.wait_ge(s, value)
            if not isinstance(value, int):
                eng.sem_inc(waits_carried, 1)

        def quart(t, n):
            return t[:, QT * (QUARTS - 1 - n):QT * (QUARTS - n)]

        block = ctx.enter_context(nc.Block())

        @block.sync
        def _(sp):
            def load(g, c, again):
                for h in range(CH):
                    if again:
                        wait_apart(sp, mask_ready[h], UNITS * g + c - RING + 1)
                    j0 = N - COLS * (c + 1)
                    sp.dma_start(adj_ring[:, c % RING, h], adj_v[g, h, :, :, j0:j0 + COLS])\
                      .then_inc(load_done[c % RING][h], 16)

            def load_x(n):
                t0 = QT * (QUARTS - 1 - n)
                sp.dma_start(xs[:, t0:t0 + QT].rearrange("p (s t) d -> p s t d", t=CT),
                             x_v[:, t0 // CT:(t0 + QT) // CT]).then_inc(x_loaded[n], 16)

            for c in range(UNITS):
                if c < 2:
                    load_x(c)
                load(0, c, c >= RING)
                if 2 <= c < QUARTS:
                    load_x(c)
            sp.dma_start(bias_sb[:], bias_v.broadcast_to([P, D])).then_inc(bias_loaded, 16)
            with sp.Fori(1, GROUPS) as g:
                for c in range(UNITS):
                    load(g, c, True)
            for h in range(CH):
                sp.wait_ge(out_ready[h], GROUPS)
                t0 = CH * CT * (GROUPS - 1) + CT * h
                sp.dma_start(out_v[GROUPS - 1, h], out_sb[:, t0:t0 + CT]).then_inc(last_stored[h], 16)
            for h in range(CH):
                sp.wait_ge(last_stored[h], 16)

        @block.gpsimd
        def _(pool):
            steps = [0]

            def then_next(ins):
                steps[0] += 1
                ins.then_inc(pool_step, 1)
                pool.wait_ge(pool_step, steps[0])

            def fill_where(t, keep, base, step, cm, fill):
                return nc.gpsimd.affine_select(out=t, in_=t, compare_op=keep, fill=fill, base=base,
                                               pattern=[[step, t.shape[1]]], channel_multiplier=cm)

            then_next(nc.gpsimd.memset(ident[:], 0.0))
            fill_where(ident[:], ALU.not_equal, 0, -1, 1, 1.0).then_inc(ident_set, 1)
            then_next(nc.gpsimd.memset(this_block[:], 0.0))
            then_next(fill_where(this_block[:], ALU.is_ge, 0, 1, -1, -EXP_ONE / SET))
            then_next(fill_where(this_block[:], ALU.not_equal, 0, 1, -1, DROP / SET))
            then_next(nc.gpsimd.memset(to_left[:], -EXP_ONE / SET))
            then_next(fill_where(to_left[:], ALU.is_ge, 0, 1, -1, 0.0))
            fill_where(to_left[:], ALU.not_equal, 0, 1, -1, -(EXP_ONE + DROP) / SET).then_inc(count_mats_set, 1)
            then_next(nc.gpsimd.memset(ident16[:], 0.0))
            fill_where(ident16[:], ALU.not_equal, 0, -1, 1, 1.0).then_inc(ident16_set, 1)

            def centre(n):
                pool.wait_ge(x_loaded[n], 16)
                pool.wait_ge(mean_set, n + 1)
                nc.gpsimd.tensor_tensor(quart(cen, n), quart(xs, n),
                                        quart(mean, n).unsqueeze(2).broadcast_to([P, QT, D]),
                                        ALU.subtract).then_inc(centred, 1)

            def normalise(n):
                pool.wait_ge(rstd0_set, n + 1)
                then_next(nc.gpsimd.tensor_tensor(quart(nw1, n), quart(rstd0, n), quart(rstd0, n), ALU.mult))
                pool.wait_ge(var_set, n + 1)
                then_next(nc.gpsimd.tensor_tensor(quart(nw2, n), quart(nw1, n), quart(var, n), ALU.mult))
                then_next(nc.gpsimd.tensor_scalar(quart(nw3, n), quart(nw2, n), -0.5 * 2 ** H_BITS, 1.5 * 2 ** H_BITS,
                                                  ALU.mult, ALU.add))
                then_next(nc.gpsimd.tensor_tensor(quart(rstd, n), quart(rstd0, n), quart(nw3, n), ALU.mult))
                nc.gpsimd.tensor_tensor(quart(h_sb, n), quart(cen, n),
                                        quart(rstd, n).unsqueeze(2).broadcast_to([P, QT, D]),
                                        ALU.mult).then_inc(h_set, 1)

            for n in range(QUARTS):
                centre(n)
                normalise(n)
            pool.wait_ge(bias_loaded, 16)
            nc.gpsimd.tensor_tensor(out_sb[:], xs[:], bias_sb[:].unsqueeze(1).broadcast_to([P, TILES, D]),
                                    ALU.add).then_inc(out_begun, 1)
            for g in range(GROUPS - 1):
                for h in range(CH):
                    pool.wait_ge(out_ready[h], g + 1)
                    t0 = CH * CT * g + CT * h
                    pool.dma_start(out_v[g, h], out_sb[:, t0:t0 + CT]).then_inc(out_stored[h], 16)
            for h in range(CH):
                pool.wait_ge(out_stored[h], 16 * (GROUPS - 1))

        @block.scalar
        def _(act):
            def weights(g, c, k):
                for h in range(CH):
                    act.wait_ge(count_ready[h], EB * (UNITS * g + c) + k + 1)
                    nc.scalar.activation(wts[:, h, EB * (c % 2) + k, :], count_ps[h][:], ACT.Relu,
                                         bias=float(BIAS - DROP)).then_inc(wts_ready[h], 1)

            def square(n):
                act.wait_ge(centred, n + 1)
                nc.scalar.activation(quart(sq, n), quart(cen, n), ACT.Square).then_inc(squared, 1)

            def root(n):
                act.wait_ge(var_set, n + 1)
                nc.scalar.activation(quart(std, n), quart(var, n), ACT.Sqrt).then_inc(std_set, 1)

            def high_half(n):
                act.wait_ge(h_set, n + 1)
                nc.scalar.activation(quart(halves, n)[:, :, 0, :], quart(h_sb, n), ACT.Relu).then_inc(high_set, 1)

            def low_half(n):
                act.wait_ge(rest_set, n + 1)
                nc.scalar.activation(quart(halves, n)[:, :, 1, :], quart(rest, n), ACT.Copy,
                                     scale=float(2 ** HALF_BITS)).then_inc(halves_set, 1)

            def copy_h_t(n):
                act.wait_ge(h_turned, n + 1)
                c0 = P * QT * (QUARTS - 1 - n)
                nc.scalar.activation(h_t[:, c0:c0 + P * QT].rearrange("d (s p t) -> d s t p", s=QT // CT, p=P),
                                     rows_ps[0][:].bitcast(F16).rearrange("d (s t p) -> d s t p", s=QT // CT, t=CT),
                                     ACT.Copy).then_inc(h_t_set, 1)

            for half in range(2):
                act.dma_start(w_out[half * D:(half + 1) * D], weight).then_inc(w_loaded, 16)
            act.preload_act_table(ACT.Sqrt)
            act.wait_ge(w_loaded, 2 * 16)
            for half in range(2):
                rows = w_out[half * D:(half + 1) * D]
                nc.scalar.activation(rows, rows, ACT.Copy, scale=2.0 ** (OUT_BITS - H_BITS - HALF_BITS * half))\
                  .then_inc(w_out_set, 1)
            square(0)
            root(0)
            high_half(0)
            low_half(0)
            for c in range(UNITS + 1):
                new, split, turned = (c + 2) // 2, (c + 1) // 2, c // 2
                for k in range(EB):
                    weights(0, c, k)
                    if c % 2 == 0 and new < QUARTS and k in (1, 2):
                        (square, root)[k - 1](new)
                    if c % 2 and split < QUARTS and k in (1, 3):
                        (high_half, low_half)[k // 2](split)
                    if c % 2 == 0 and turned < QUARTS and k == 0:
                        copy_h_t(turned)
            with act.Fori(1, GROUPS - 1) as g:
                for c in range(1, UNITS + 1):
                    for k in range(EB):
                        weights(g, c, k)
            for c in range(1, UNITS):
                for k in range(EB):
                    weights(GROUPS - 1, c, k)
            act.wait_ge(rows_ready[1], GROUPS - 1)
            act.wait_ge(product_done[1], TILES * GROUPS)
            nc.scalar.activation(acc_sb[:, 1], acc_ps[1][:], ACT.Copy).then_inc(acc_copied[1], 1)

        @block.vector
        def _(dve):
            steps = [0]

            def then_next(ins):
                steps[0] += 1
                ins.then_inc(dve_step, 1)
                dve.wait_ge(dve_step, steps[0])

            def make_mask(g, c, h):
                wait_apart(dve, load_done[c % RING][h], 16 * ((UNITS // RING) * g + c // RING + 1))
                src = adj_ring[:, c % RING, h].rearrange("p t (e q) -> p t e q", e=EB)
                dst = mask[:, c % 2, h].rearrange("p t (q e) -> p t e q", e=EB)
                nc.vector.tensor_scalar(dst, src, 0.0, SET, ALU.not_equal, ALU.mult, saturate=False)\
                  .then_inc(mask_ready[h], 1)

            def pack(g, c):
                u = UNITS * g + c
                for h in range(CH):
                    dve.wait_ge(mask_ready[h], u + 1)
                if not (g is 0 and c < 2):
                    dve.wait_ge(words_ready, u - 1)
                tiles = mask[:, c % 2].rearrange("p h (a b) n -> p (h a) b n", b=2).bitcast(U32)
                nc.vector.scalar_tensor_tensor(out=pairs[:].rearrange("p h a q -> p (h a) q"),
                                               in0=tiles[:, :, 1], scalar=1, in1=tiles[:, :, 0],
                                               op0=ALU.logical_shift_right, op1=ALU.bitwise_or)\
                  .then_inc(pairs_ready, 1)
                dve.wait_ge(pairs_ready, u + 1)
                nc.vector.scalar_tensor_tensor(out=packed[:, c % 2], in0=pairs[:, :, 1], scalar=2,
                                               in1=pairs[:, :, 0], op0=ALU.logical_shift_right,
                                               op1=ALU.bitwise_or).then_inc(packed_ready, 1)

            def unpack(g, c):
                dve.wait_ge(words_ready, UNITS * g + c + 1)
                words = words_ps[c % 2][:, 0:CH * P].bitcast(U32).rearrange("p (h i) -> p h i", i=P)
                tiles = mask_t[:, c % 2].rearrange("p h (t i) e -> p h t (i e)", t=CT).bitcast(U32)
                for t in range(CT):
                    ins = nc.vector.tensor_scalar(tiles[:, :, t], words, t, BYTES_BIT, ALU.logical_shift_left,
                                                  ALU.bitwise_and)
                ins.then_inc(mask_t_ready, 1)

            def copy_sums(g, chains):
                for h in chains:
                    dve.wait_ge(product_done[h], TILES * (g + 1))
                    nc.vector.tensor_copy(acc_sb[:, h], acc_ps[h][:]).then_inc(acc_copied[h], 1)

            def add_rows(g):
                for h in range(CH):
                    dve.wait_ge(rows_ready[h], g + 1)
                    rows = rows_ps[h][:, 0:CT * D].rearrange("p (t d) -> p t d", t=CT)
                    place = out_sb[:, bass.ds(CH * CT * g + CT * h, CT), :]
                    nc.vector.tensor_tensor(place, rows, place, ALU.add).then_inc(out_ready[h], 1)

            def means(n):
                dve.wait_ge(x_loaded[n], 16)
                then_next(nc.vector.tensor_reduce(quart(row_sum, n), quart(xs, n), AX.X, ALU.add))
                nc.vector.tensor_scalar(quart(mean, n), quart(row_sum, n), 1.0 / D, None, ALU.mult)\
                  .then_inc(mean_set, 1)

            def variances(n):
                dve.wait_ge(squared, n + 1)
                then_next(nc.vector.tensor_reduce(quart(sq_sum, n), quart(sq, n), AX.X, ALU.add))
                nc.vector.tensor_scalar(quart(var, n), quart(sq_sum, n), 1.0 / D, EPS, ALU.mult, ALU.add)\
                  .then_inc(var_set, 1)

            def reciprocals(n):
                dve.wait_ge(std_set, n + 1)
                nc.vector.reciprocal(quart(rstd0, n), quart(std, n)).then_inc(rstd0_set, 1)

            def leave_rest(n):
                dve.wait_ge(high_set, n + 1)
                nc.vector.scalar_tensor_tensor(out=quart(rest, n), in0=quart(h_sb, n), scalar=0.0,
                                               in1=quart(halves, n)[:, :, 0, :], op0=ALU.max,
                                               op1=ALU.subtract).then_inc(rest_set, 1)

            def copy_h_rows(n):
                dve.wait_ge(h_back, n + 1)
                nc.vector.tensor_copy(quart(h_rows, n).rearrange("p t s d -> p (t s d)"), rows_ps[1][:].bitcast(F16))\
                  .then_inc(h_rows_set, 1)

            def stage(g, c, first=False):
                new, split, turned = (c + 2) // 2, (c + 1) // 2, c // 2
                entering = first and c % 2 == 0 and new < QUARTS
                last = g is GROUPS - 1
                if entering:
                    means(new)
                if not (last and c + 2 >= UNITS):
                    make_mask(g, c + 2, 0)
                if not (last and c + 1 >= UNITS):
                    unpack(g, c + 1)
                if entering:
                    variances(new)
                if first and c % 2 and split < QUARTS:
                    leave_rest(split)
                if first and c % 2 == 0 and 0 < turned < QUARTS:
                    copy_h_rows(turned)
                if entering:
                    reciprocals(new)
                if c == UNITS:
                    copy_sums(g, range(CH))
                if not (last and c + 2 >= UNITS):
                    make_mask(g, c + 2, 1)
                    pack(g, c + 2)
                if c == 1 and not first:
                    add_rows(g - 1)

            means(0)
            make_mask(0, 0, 0)
            variances(0)
            reciprocals(0)
            make_mask(0, 0, 1)
            pack(0, 0)
            leave_rest(0)
            unpack(0, 0)
            means(1)
            for h in range(CH):
                make_mask(0, 1, h)
            pack(0, 1)
            variances(1)
            unpack(0, 1)
            reciprocals(1)
            copy_h_rows(0)
            for h in range(CH):
                make_mask(0, 2, h)
            pack(0, 2)
            for c in range(1, UNITS):
                stage(0, c, True)
            dve.wait_ge(out_begun, 1)
            stage(0, UNITS, True)
            with dve.Fori(1, GROUPS - 1) as g:
                for c in range(1, UNITS + 1):
                    stage(g, c)
            for c in range(1, UNITS):
                stage(GROUPS - 1, c)
            copy_sums(GROUPS - 1, [0])
            add_rows(GROUPS - 1)

        @block.tensor
        def _(pe):
            def turn_words(g, c):
                pe.wait_ge(packed_ready, UNITS * g + c + 1)
                for h in range(CH):
                    ins = nc.tensor.transpose(words_ps[c % 2][:, h * P:(h + 1) * P],
                                              packed[:, c % 2, h].bitcast(F32), ident[:])
                ins.then_inc(words_ready, 1)

            def masks_of(c, h, k):
                return mask_t[:, c % 2, h, :, EB - 1 - k]

            def count(g, c, k, h):
                u = UNITS * g + c
                first = c % UNITS == 0 and k == 0
                if not (g is 0 and c == 0 and first):
                    wait_apart(pe, wts_ready[h], EB * u + k)
                if not first:
                    pc, pk = (c, k - 1) if k else (c - 1, EB - 1)
                    nc.tensor.matmul(count_ps[h][:], to_left[:], masks_of(pc, h, pk), start=False, stop=True,
                                     skip_group_check=True)
                if k == 0 and h == 0:
                    wait_apart(pe, mask_t_ready, u + 1)
                nc.tensor.matmul(count_ps[h][:], this_block[:], masks_of(c, h, k), start=first, stop=True,
                                 skip_group_check=True).then_inc(count_ready[h], 1)

            def product(g, c, k, h):
                if c == 0 and k == 0:
                    if g is not 0:
                        pe.wait_ge(acc_copied[h], g)
                pe.wait_ge(wts_ready[h], EB * (UNITS * g + c) + k + 1)
                if g is 0 and c % 2 == 0 and k == 0:
                    pe.wait_ge(h_rows_set, c // 2 + 1)
                b = TILES - 1 - EB * c - k
                nc.tensor.matmul(acc_ps[h][:], h_rows[:, b].rearrange("p s d -> p (s d)"),
                                 wts[:, h, EB * (c % 2) + k, :].bitcast(BF16),
                                 start=(c == 0 and k == 0), stop=(c == UNITS - 1 and k == EB - 1))\
                  .then_inc(product_done[h], 1)

            def turn_h(n):
                pe.wait_ge(halves_set, n + 1)
                if n:
                    pe.wait_ge(h_t_set, n)
                turned = rows_ps[0][:].bitcast(F16)
                for a in range(QT):
                    ins = nc.tensor.transpose(turned[:, a * P:(a + 1) * P],
                                              quart(halves, n)[:, a].rearrange("p s d -> p (s d)"), ident16[:])
                ins.then_inc(h_turned, 1)

            def turn_back(n):
                pe.wait_ge(h_t_set, n + 1)
                if n:
                    pe.wait_ge(h_rows_set, n)
                back = rows_ps[1][:].bitcast(F16)
                for a in range(QT):
                    j = P * (QT * (QUARTS - 1 - n) + a)
                    ins = nc.tensor.transpose(back[:, a * P:(a + 1) * P], h_t[:, j:j + P], ident16[:])
                ins.then_inc(h_back, 1)

            def unit(g, c, first=False):
                closing = c == UNITS
                turned = c // 2
                for k in range(EB):
                    for h in range(CH):
                        count(g, c, k, h)
                        for kk in ([[0, 1], [2], [3], []][k] if closing else [k]) if c else []:
                            product(g, c - 1, kk, h)
                        if k == 2 and h == 0 and not (g is GROUPS - 1 and c == UNITS - 1):
                            turn_words(g, c + 1)
                    if first and c == 0 and k == 1:
                        turn_back(0)
                    if k == 1 and c == 1 and not first:
                        to_rows(g - 1)
                    if first and c and c % 2 == 0 and turned < QUARTS:
                        if k == 0:
                            turn_h(turned)
                        if k == 2:
                            turn_back(turned)

            def to_rows(g):
                for h in range(CH):
                    pe.wait_ge(acc_copied[h], g + 1)
                    for t in range(CT):
                        ins = nc.tensor.matmul(rows_ps[h][:, t * D:(t + 1) * D], acc_sb[:, h, t:ROWS:CT], w_out[:],
                                               start=True, stop=True, skip_group_check=True)
                    ins.then_inc(rows_ready[h], 1)

            pe.wait_ge(ident_set, 1)
            pe.wait_ge(count_mats_set, 1)

            def warm_up(products):
                for _ in range(products):
                    nc.tensor.matmul(count_ps[0][:], to_left[:], to_left[:].unsqueeze(1).broadcast_to([P, 4, P]),
                                     start=True, stop=True, skip_group_check=True)

            warm_up(24)
            turn_words(0, 0)
            pe.wait_ge(ident16_set, 1)
            warm_up(4)
            turn_h(0)
            warm_up(3)
            for c in range(UNITS):
                unit(0, c, first=True)
            pe.wait_ge(w_out_set, 2)
            unit(0, UNITS, first=True)
            with pe.Fori(1, GROUPS - 1) as g:
                for c in range(1, UNITS + 1):
                    unit(g, c)
            for c in range(1, UNITS):
                unit(GROUPS - 1, c)
            for h in range(CH):
                for k in range(EB):
                    product(GROUPS - 1, UNITS - 1, k, h)
            to_rows(GROUPS - 1)


def kernel(x, adj, L0_gnn_weight, L0_gnn_bias):
    import numpy as np
    import concourse.bacc as bacc
    from concourse.bass_utils import run_bass_kernel_spmd

    nc = bacc.Bacc("TRN2", target_bir_lowering=False, num_devices=1)
    ins = {"x": x, "adj": adj, "weight": L0_gnn_weight, "bias": L0_gnn_bias}
    arrays = {f"in_{n}": np.ascontiguousarray(a) for n, a in ins.items()}
    args = [nc.dram_tensor(n, a.shape, mybir.dt.from_np(a.dtype), kind="ExternalInput").ap()
            for n, a in arrays.items()]
    out = nc.dram_tensor("out", x.shape, F32, kind="ExternalOutput").ap()
    neighbour_decay_kernel(nc, *args, out)
    r = run_bass_kernel_spmd(nc, [arrays], core_ids=[0])
    return r.results[0]["out"]
```
